# Optimizing a Trainium2 kernel written in Bass

```python
import numpy as np
import jax
import jax.numpy as jnp

def _softmax(x, axis=-1):
    return jax.nn.softmax(x, axis=axis)

def _gelu(x):
    return jax.nn.gelu(x, approximate=True)

def _silu(x):
    return jax.nn.silu(x)

def _sigmoid(x):
    return jax.nn.sigmoid(x)

def _layernorm(x, axis=-1, eps=1e-05):
    m = jnp.mean(x, axis=axis, keepdims=True)
    v = jnp.var(x, axis=axis, keepdims=True)
    return (x - m) / jnp.sqrt(v + eps)

def _scatter_add(tgt, idx, src, axis=0):
    return tgt.at[idx].add(src)

def _segment_sum(src, seg, n):
    return jax.ops.segment_sum(src, seg, n)
kernel_name = 'mk_seq_postln_d1_jaxref_r4_63a783'

def setup_inputs(seed: int=0):
    np.random.seed(seed)
    _w = jnp.asarray

    def _L0_attn_setup():
        import jax, jax.numpy as jnp
        import numpy as np
        import math
        D_MODEL = 256
        NHEAD = 16
        FACTOR = 5
        key = jax.random.key(seed)
        ks = jax.random.split(key, 9)
        d = D_MODEL
        s = 1.0 / math.sqrt(d)
        x = jax.random.normal(ks[0], (2, 512, d), dtype=jnp.float32)
        Wq = jax.random.normal(ks[1], (d, d), dtype=jnp.float32) * s
        bq = jnp.zeros((d,), dtype=jnp.float32)
        Wk = jax.random.normal(ks[2], (d, d), dtype=jnp.float32) * s
        bk = jnp.zeros((d,), dtype=jnp.float32)
        Wv = jax.random.normal(ks[3], (d, d), dtype=jnp.float32) * s
        bv = jnp.zeros((d,), dtype=jnp.float32)
        Wo = jax.random.normal(ks[4], (d, d), dtype=jnp.float32) * s
        bo = jnp.zeros((d,), dtype=jnp.float32)
        return {'x': x, 'Wq': Wq, 'bq': bq, 'Wk': Wk, 'bk': bk, 'Wv': Wv, 'bv': bv, 'Wo': Wo, 'bo': bo}
    _L0_attn_in = _L0_attn_setup()

    def _L0_ffn_setup():
        import jax, jax.numpy as jnp
        import numpy as np
        DIM = 256
        HIDDEN = 768
        SCALE = 1.0 / 127.0

        def _dequant(w_int, dtype):
            return w_int.astype(dtype) * jnp.asarray(SCALE, dtype)
        key = jax.random.key(seed)
        k_x, k_g, k_u, k_d = jax.random.split(key, 4)
        x = jax.random.normal(k_x, (4, 512, DIM), dtype=jnp.float32)
        w_gate = jax.random.randint(k_g, (HIDDEN, DIM), -127, 128, dtype=jnp.int32)
        w_up = jax.random.randint(k_u, (HIDDEN, DIM), -127, 128, dtype=jnp.int32)
        w_down = jax.random.randint(k_d, (DIM, HIDDEN), -127, 128, dtype=jnp.int32)
        return {'x': x, 'w_gate': w_gate, 'w_up': w_up, 'w_down': w_down}
    _L0_ffn_in = _L0_ffn_setup()
    _d = {'L0_attn_x': _L0_attn_in['x'], 'L0_attn_Wq': _L0_attn_in['Wq'], 'L0_attn_bq': _L0_attn_in['bq'], 'L0_attn_Wk': _L0_attn_in['Wk'], 'L0_attn_bk': _L0_attn_in['bk'], 'L0_attn_Wv': _L0_attn_in['Wv'], 'L0_attn_bv': _L0_attn_in['bv'], 'L0_attn_Wo': _L0_attn_in['Wo'], 'L0_attn_bo': _L0_attn_in['bo'], 'L0_ffn_w_gate': _L0_ffn_in['w_gate'], 'L0_ffn_w_up': _L0_ffn_in['w_up'], 'L0_ffn_w_down': _L0_ffn_in['w_down']}
    _x0 = _d['L0_attn_x']
    _d['L0_attn_x'] = jax.random.normal(jax.random.fold_in(jax.random.key(seed), 1), (16, 512, 256), dtype=_x0.dtype)
    del _x0
    return _d

def reference(L0_attn_x, L0_attn_Wq, L0_attn_bq, L0_attn_Wk, L0_attn_bk, L0_attn_Wv, L0_attn_bv, L0_attn_Wo, L0_attn_bo, L0_ffn_w_gate, L0_ffn_w_up, L0_ffn_w_down):

    def _L0_attn_ref(x, Wq, bq, Wk, bk, Wv, bv, Wo, bo):
        import jax, jax.numpy as jnp
        import numpy as np
        import math
        D_MODEL = 256
        NHEAD = 16
        FACTOR = 5
        B, L, d_model = x.shape
        H = NHEAD
        D = d_model // H
        U = min(L, int(FACTOR * math.log(L)))

        def proj(W, b):
            return (x @ W.T + b).reshape(B, L, H, D).transpose(0, 2, 1, 3)
        Q = proj(Wq, bq)
        K = proj(Wk, bk)
        V = proj(Wv, bv)
        scores = jnp.einsum('bhqd,bhkd->bhqk', Q, K) / math.sqrt(D)
        top_vals, _ = jax.lax.top_k(scores, U)
        thresh = top_vals[..., -1:]
        scores = jnp.where(scores < thresh, -jnp.inf, scores)
        attn = jax.nn.softmax(scores, axis=-1)
        context = jnp.einsum('bhqk,bhkd->bhqd', attn, V)
        context = context.transpose(0, 2, 1, 3).reshape(B, L, d_model)
        return context @ Wo.T + bo

    def _L0_ffn_ref(x, w_gate, w_up, w_down):
        import jax, jax.numpy as jnp
        import numpy as np
        DIM = 256
        HIDDEN = 768
        SCALE = 1.0 / 127.0

        def _dequant(w_int, dtype):
            return w_int.astype(dtype) * jnp.asarray(SCALE, dtype)
        wg = _dequant(w_gate, x.dtype)
        wu = _dequant(w_up, x.dtype)
        wd = _dequant(w_down, x.dtype)
        gate = jnp.einsum('bsd,hd->bsh', x, wg)
        up = jnp.einsum('bsd,hd->bsh', x, wu)
        h = jax.nn.silu(gate) * up
        return jnp.einsum('bsh,dh->bsd', h, wd)
    x = L0_attn_x
    x = _layernorm(x + _L0_attn_ref(x, L0_attn_Wq, L0_attn_bq, L0_attn_Wk, L0_attn_bk, L0_attn_Wv, L0_attn_bv, L0_attn_Wo, L0_attn_bo), axis=-1)
    x = _layernorm(x + _L0_ffn_ref(x, L0_ffn_w_gate, L0_ffn_w_up, L0_ffn_w_down), axis=-1)
    return x

_drawn_inputs = setup_inputs


def setup_inputs(seed=0):
    import zlib

    import numpy as np

    out = dict(_drawn_inputs(seed))
    spreads = {'L0_attn_bq': (0.0, 0.1),
     'L0_attn_bk': (0.0, 0.1),
     'L0_attn_bv': (0.0, 0.1),
     'L0_attn_bo': (0.0, 0.1)}
    factors = {}
    for name, (base, spread) in spreads.items():
        noise = np.random.default_rng([zlib.crc32(name.encode()), seed]).standard_normal(out[name].shape)
        drawn = base * np.exp(spread * noise) if base else spread * noise
        out[name] = jnp.asarray(drawn.astype(out[name].dtype))
    for name, factor in factors.items():
        out[name] = (out[name] * factor).astype(out[name].dtype)
    return out
```

```python
from contextlib import ExitStack

import numpy as np

import concourse.bass as bass
from concourse import mybir

B, L, DM = 16, 512, 256
H, D = 16, 16
HID = 768
TOP = 31
P = 128
C = DM // P
NT = L // P
HG = P // 32
NG = H // HG
NF = HID // P
VW = 32
PAIRS = H * NT // 2
GP = PAIRS // NG
TILES = 2 * PAIRS
SCALE = float(D) ** -0.5
DEQ = float(np.float32(1.0 / 127.0))
EPS = 1e-5
GONE = -3.0e38

CTX_T, OUT_PROJ, X1_T, FFN0, DOWN = 3, 4, 6, 7, 19
FFN_SLOTS = {FFN0 + 2 * f: f for f in range(NF)}
PROJ_SLOTS = {3: 0, 4: 1, 5: 2}
CTX_SLOT = 2

F32 = mybir.dt.float32
I32 = mybir.dt.int32
ALU = mybir.AluOpType
ACT = mybir.ActivationFunctionType


def pair_place(j):
    grp, r = divmod(j, GP)
    return grp, r // 2, 2 * (r % 2)


def build(nc, xT, x, wqT, wkT, wvT, woT, bq, bk, bv, bo, wgT, wuT, wdT, ident_in, out):
    with ExitStack() as ctx:
        def sb(name, shape, dt=F32):
            return ctx.enter_context(nc.sbuf_tensor(name, shape, dt))

        def ps(name, shape):
            return ctx.enter_context(nc.psum_tensor(name, shape, F32))

        def sem(name):
            return ctx.enter_context(nc.semaphore(name))

        ident = sb("ident", [P, P])
        ones = sb("ones", [1, P])
        wqk = [sb(f"w{n}", [P, C, NG, HG, 32]) for n in "qk"]
        bqk = [sb(f"b{n}", [P, NG]) for n in "qk"]
        wv = sb("wv", [P, C, DM])
        wo = sb("wo", [P, C, DM])
        bvr = sb("bvr", [1, DM])
        bor = sb("bor", [1, DM])
        wint = sb("wint", [P, 3, C * HID], I32)
        wg = sb("wg", [P, C, HID])
        wu = sb("wu", [P, C, HID])
        wd = sb("wd", [P, NF, DM])
        minus_half = sb("minus_half", [P, NT])

        xTs = sb("xTs", [P, C, L])
        xs = sb("xs", [P, NT, DM])
        QKT = [sb(f"{n}T", [P, NG, L]) for n in "QK"]
        V = sb("V", [P, NT, H, VW])
        ctxs = sb("ctxs", [P, NT, H, D])
        ctxr = sb("ctxr", [P, L])
        rden = sb("rden", [P, NT, HG])
        ctxT = sb("ctxT", [P, C, L])
        res = sb("res", [P, NT, DM])
        stats = sb("stats", [P, NT, 6])
        mv = sb("mv", [P, NT, 2])
        veps = sb("veps", [P, NT])
        rstd = sb("rstd", [P, NT])
        x1 = sb("x1", [P, NT, DM])
        x1T = sb("x1T", [P, C, L])
        th = sb("th", [P, L])
        hgs = sb("hgs", [P, L])
        hT = sb("hT", [P, NF, L])
        outs = sb("outs", [P, NT, DM])

        S = sb("S", [P, 4, 2, L])
        W = sb("W", [P, 2, L])
        top = sb("top", [P, 4, 2, 32])
        nmax = sb("nmax", [P, 4, 2])
        E = sb("E", [P, 2, 2, L])
        keep = sb("keep", [P, 2, L])
        Pm = sb("Pm", [P, 2, 2, L])
        PT = sb("PT", [P, 2, 2, L])

        S_ps = [ps(f"S_ps{a}", [P, L]) for a in range(2)]
        PT_ps = [ps(f"PT_ps{a}", [P, L]) for a in range(2)]
        ctxT_ps = ps("ctxT_ps", [P, L])
        side_ps = [ps(f"side_ps{a}", [P, L]) for a in range(2)]
        work_ps = ps("work_ps", [P, L])

        w_loaded = sem("w_loaded")
        ffn_loaded = sem("ffn_loaded")
        xT_loaded = sem("xT_loaded")
        x_loaded = sem("x_loaded")
        pads_zero = sem("pads_zero")
        consts_done = sem("consts_done")
        deq_done = sem("deq_done")
        proj_done = sem("proj_done")
        proj_copied = sem("proj_copied")
        scores_done = sem("scores_done")
        s_copied = sem("s_copied")
        max_done = sem("max_done")
        dve_step = sem("dve_step")
        thr_done = sem("thr_done")
        nmax_done = sem("nmax_done")
        exp_done = sem("exp_done")
        keep_done = sem("keep_done")
        p_done = sem("p_done")
        pT_done = sem("pT_done")
        pT_copied = sem("pT_copied")
        pv_done = sem("pv_done")
        raw_copied = sem("raw_copied")
        turned_done = sem("turned_done")
        rden_done = sem("rden_done")
        ctx_taken = sem("ctx_taken")
        ctxT_done = sem("ctxT_done")
        ctxT_copied = sem("ctxT_copied")
        oproj_done = sem("oproj_done")
        res_done = sem("res_done")
        stats_done = sem("stats_done")
        mv_done = sem("mv_done")
        ln_step = sem("ln_step")
        x1_done = sem("x1_done")
        x1T_done = sem("x1T_done")
        x1T_copied = sem("x1T_copied")
        gate_done = sem("gate_done")
        th_done = sem("th_done")
        hg_done = sem("hg_done")
        h_done = sem("h_done")
        down_done = sem("down_done")
        out_done = sem("out_done")
        stored = sem("stored")

        N_W = 14
        block = ctx.enter_context(nc.Block())

        def wait_apart(eng, s, value):
            eng.wait_ge(s, value)
            eng.nop(nofuse=True)


        @block.sync
        def _(sp):
            def load_xT(b):
                sp.dma_start(xTs[:, :, :], xT[b].rearrange("(c p) t -> p c t", p=P)).then_inc(xT_loaded, 16)

            def load_x(b):
                sp.dma_start(xs[:, :, :], x[b].rearrange("(n p) d -> p n d", p=P)).then_inc(x_loaded, 16)

            def store(b):
                sp.dma_start(out[b].rearrange("(n p) d -> p n d", p=P), outs[:, :, :]).then_inc(stored, 16)

            load_xT(0)
            sp.wait_ge(pads_zero, 4)
            for w, src in ((0, wqT), (1, wkT)):
                for c in range(C):
                    sp.dma_start(wqk[w][:, c, :, :, 0:D],
                                 src[c * P:(c + 1) * P, :].rearrange("p (g s d) -> p g s d", g=NG, s=HG)
                                 ).then_inc(w_loaded, 16)
            for w, src in ((0, bq), (1, bk)):
                for i in range(HG):
                    sp.dma_start(bqk[w][32 * i:32 * i + D, :],
                                 src[i]).then_inc(w_loaded, 16)
            sp.dma_start(wv[:, :, :], wvT.rearrange("(c p) n -> p c n", p=P)).then_inc(w_loaded, 16)
            sp.dma_start(bvr[:, :], bv.rearrange("(a n) -> a n", a=1)).then_inc(w_loaded, 16)
            load_x(0)

            def steps(b, last):
                sp.wait_ge(proj_done, b * 12 + 12)
                load_xT(b if last else b + 1)
                sp.wait_ge(res_done, b * 4 - 2)
                load_x(b)
                sp.wait_ge(out_done, b * NT)
                store(b - 1)

            sp.wait_ge(proj_done, 12)
            load_xT(1)
            with sp.Fori(1, B - 1) as b:
                steps(b, False)
            steps(B - 1, True)
            sp.wait_ge(out_done, B * NT)
            store(B - 1)
            sp.wait_ge(stored, 16 * (B + 1))
            sp.wait_ge(xT_loaded, 16 * (B + 1))

        @block.scalar
        def _(act):
            act.dma_start(ident[:, :], ident_in).then_inc(w_loaded, 16)
            act.dma_start(wo[:, :, :], woT.rearrange("(c p) n -> p c n", p=P)).then_inc(ffn_loaded, 16)
            act.dma_start(bor[:, :], bo.rearrange("(a n) -> a n", a=1)).then_inc(ffn_loaded, 16)
            for i, w in enumerate((wgT, wuT, wdT)):
                act.dma_start(wint[:, i, :].rearrange("p (c n) -> p c n", n=w.shape[1]),
                              w.rearrange("(c p) n -> p c n", p=P)).then_inc(ffn_loaded, 16)

            def project_copy(G, grp, what):
                act.wait_ge(proj_done, 3 * G + what + 1)
                if what < 2:
                    nc.scalar.activation(QKT[what][:, grp, :], work_ps[:, :], ACT.Identity,
                                         bias=bqk[what][:, grp:grp + 1]).then_inc(proj_copied, 1)
                else:
                    nc.scalar.activation(V[:, :, grp * HG:(grp + 1) * HG, 0:D],
                                         work_ps[:, 0:NT * HG * D].rearrange("p (n h d) -> p n h d", n=NT, h=HG),
                                         ACT.Copy).then_inc(proj_copied, 1)

            def copy_scores(T0, j, buffers_used):
                for a in range(2):
                    act.wait_ge(scores_done, T0 + a + 1)
                    if buffers_used:
                        act.wait_ge(p_done, T0 + a - 7)
                    nc.scalar.activation(S[:, j % 4, a, :], S_ps[a][:, :], ACT.Copy).then_inc(s_copied, 1)

            def slots(b, first, rest):
                for k in range(PAIRS):
                    T = b * TILES + 2 * k
                    if k % GP == CTX_SLOT and not (first and k < GP) and not (rest and k >= GP):
                        act.wait_ge(pv_done, b * PAIRS + k - CTX_SLOT)
                        nc.scalar.activation(ctxr[:, :], ctxT_ps[:, :], ACT.Copy).then_inc(raw_copied, 1)
                    if not rest:
                        copy_scores(T + 2, k + 1, not (first and k + 1 < 4))
                        for a in range(2):
                            act.wait_ge(nmax_done, T + a + 1)
                            if not (first and k < 2):
                                act.wait_ge(p_done, T + a - 3)
                            nc.scalar.activation(E[:, k % 2, a, :], S[:, k % 4, a, :], ACT.Exp,
                                                 bias=nmax[:, k % 4, a:a + 1], scale=SCALE).then_inc(exp_done, 1)
                    if (k == 0 and not first) or (k > 0 and not rest):
                        for a in range(2):
                            act.wait_ge(pT_done, T - 2 + a + 1)
                            if not (first and k < 3):
                                act.wait_ge(pv_done, b * PAIRS + k - 2)
                            nc.scalar.activation(PT[:, (k - 1) % 2, a, :], PT_ps[a][:, :],
                                                 ACT.Copy).then_inc(pT_copied, 1)
                    if not rest and k % GP in PROJ_SLOTS:
                        m = k // GP
                        project_copy(b * NG + m + 3, (m + 3) % NG, PROJ_SLOTS[k % GP])
                    if first:
                        continue
                    if k == CTX_T:
                        for i in range(2):
                            act.wait_ge(ctxT_done, b * 2 - 1 + i)
                            nc.scalar.activation(ctxT[:, :, i * 2 * P:(i + 1) * 2 * P]
                                                 .rearrange("p c (n t) -> p n c t", n=2),
                                                 side_ps[i][:, :].rearrange("p (n c t) -> p n c t", n=2, c=C),
                                                 ACT.Copy).then_inc(ctxT_copied, 1)
                    if k == X1_T:
                        for i in range(2):
                            act.wait_ge(x1T_done, b * 2 - 1 + i)
                            nc.scalar.activation(x1T[:, :, i * 2 * P:(i + 1) * 2 * P]
                                                 .rearrange("p c (n t) -> p n c t", n=2),
                                                 side_ps[i][:, :].rearrange("p (n c t) -> p n c t", n=2, c=C),
                                                 ACT.Copy).then_inc(x1T_copied, 1)
                    if k in FFN_SLOTS:
                        act.wait_ge(gate_done, (b - 1) * NF + FFN_SLOTS[k] + 1)
                        nc.scalar.activation(th[:, :], side_ps[0][:, :], ACT.Tanh, scale=0.5).then_inc(th_done, 1)

            act.wait_ge(consts_done, 3)
            act.wait_ge(w_loaded, 16 * N_W + 16)
            for G in range(3):
                for what in range(3):
                    project_copy(G, G, what)
                if G == 0:
                    copy_scores(0, 0, False)
            slots(0, True, False)
            with act.Fori(1, B) as b:
                slots(b, False, False)
            slots(B, False, True)

        @block.tensor
        def _(pe):
            def project_products(grp, what):
                if what < 2:
                    for c in range(C):
                        mm = nc.tensor.matmul(work_ps[:, :], wqk[what][:, c, grp, :, :].rearrange("p s d -> p (s d)"),
                                              xTs[:, c, :], start=(c == 0), stop=(c == C - 1))
                else:
                    n = HG * D
                    for t in range(NT):
                        o = work_ps[:, t * n:(t + 1) * n]
                        for c in range(C):
                            nc.tensor.matmul(o, xTs[:, c, t * P:(t + 1) * P], wv[:, c, grp * n:(grp + 1) * n],
                                             start=(c == 0), stop=False)
                        mm = nc.tensor.matmul(o, ones[:, :], bvr[:, grp * n:(grp + 1) * n], start=False, stop=True)
                mm.then_inc(proj_done, 1)

            def scores(T0, G, j, used):
                grp, strip, q0 = pair_place(j)
                if j % GP == 0:
                    pe.wait_ge(proj_copied, 3 * G + 2)
                for a in range(2):
                    if used:
                        pe.wait_ge(s_copied, T0 + a - 1)
                    lo = 32 * strip
                    q = (q0 + a) * P
                    nc.tensor.matmul(S_ps[a][:, :], QKT[0][lo:lo + D, grp, q:q + P], QKT[1][lo:lo + D, grp, :],
                                     start=True, stop=True, tile_position=(lo, 0)).then_inc(scores_done, 1)

            def transposes(T0, j, used):
                for a in range(2):
                    pe.wait_ge(p_done, T0 + a + 1)
                    if used:
                        pe.wait_ge(pT_copied, T0 + a - 1)
                    for n in range(NT):
                        tr = nc.tensor.transpose(PT_ps[a][:, n * P:(n + 1) * P],
                                                 Pm[:, j % 2, a, n * P:(n + 1) * P], ident[:, :])
                    tr.then_inc(pT_done, 1)

            def values(T0, G, j, first_group):
                grp, strip, q0 = pair_place(j)
                if j % GP == 0:
                    pe.wait_ge(proj_copied, 3 * G + 3)
                    if not first_group:
                        pe.wait_ge(raw_copied, G)
                pe.wait_ge(pT_copied, T0 + 2)
                for n in range(NT):
                    mm = nc.tensor.matmul(ctxT_ps[32 * strip:32 * strip + VW, q0 * P:(q0 + 2) * P],
                                          V[:, n, grp * HG + strip, :], PT[:, j % 2, :, n * P:(n + 1) * P],
                                          start=(n == 0), stop=(n == NT - 1), tile_position=(0, 32 * strip))
                mm.then_inc(pv_done, 1)

            def turn_context(G):
                pe.wait_ge(raw_copied, G)
                pe.wait_ge(proj_copied, 3 * (G + 3))
                for n in range(NT):
                    tr = nc.tensor.transpose(work_ps[:, n * P:(n + 1) * P], ctxr[:, n * P:(n + 1) * P], ident[:, :])
                tr.then_inc(turned_done, 1)

            def slots(b, first, rest):
                for k in range(PAIRS):
                    T = b * TILES + 2 * k
                    if not rest:
                        nj = (k + 1) % PAIRS
                        scores(T + 2, b * NG + (k + 1) // GP, nj, True)
                    if (k < 2 and not first) or (k >= 2 and not rest):
                        j = (k - 2) % PAIRS
                        values(T - 4, b * NG + (k - 2) // GP, j, first and k == 2)
                    if k % GP == CTX_SLOT and not (first and k < GP) and not (rest and k >= GP):
                        turn_context(b * NG + k // GP)
                    if not rest and k % GP in PROJ_SLOTS:
                        m, what = k // GP, PROJ_SLOTS[k % GP]
                        if what == 0 and not (first and m == 0):
                            pe.wait_ge(ctx_taken, b * NG + m)
                        if what == 0:
                            pe.wait_ge(xT_loaded, (b + 1 + (m > 0)) * 16)
                        pe.wait_ge(proj_copied, (b * NG + m + 3) * 3 + what)
                        project_products((m + 3) % NG, what)
                    if not first:
                        tail(b, k)
                    if (k == 0 and not first) or (k > 0 and not rest):
                        transposes(T - 2, (k - 1) % PAIRS, not (first and k == 1))

            def tail(b, k):
                if k == CTX_T:
                    pe.wait_ge(ctx_taken, b * NG)
                    for i in range(2):
                        for n in range(2):
                            for c in range(C):
                                tr = nc.tensor.transpose(
                                    side_ps[i][:, (n * C + c) * P:(n * C + c + 1) * P],
                                    ctxs[:, 2 * i + n, c * P // D:(c + 1) * P // D, :].rearrange("p h d -> p (h d)"),
                                    ident[:, :])
                        tr.then_inc(ctxT_done, 1)
                if k == OUT_PROJ:
                    for i in range(2):
                        pe.wait_ge(ctxT_copied, b * 2 - 1 + i)
                        for n in range(2):
                            t = 2 * i + n
                            o = side_ps[i][:, n * DM:(n + 1) * DM]
                            for c in range(C):
                                nc.tensor.matmul(o, ctxT[:, c, t * P:(t + 1) * P], wo[:, c, :],
                                                 start=(c == 0), stop=False)
                            mm = nc.tensor.matmul(o, ones[:, :], bor[:, :], start=False, stop=True)
                        mm.then_inc(oproj_done, 1)
                if k == X1_T:
                    pe.wait_ge(x1_done, b * NT)
                    for i in range(2):
                        for n in range(2):
                            for c in range(C):
                                tr = nc.tensor.transpose(side_ps[i][:, (n * C + c) * P:(n * C + c + 1) * P],
                                                         x1[:, 2 * i + n, c * P:(c + 1) * P], ident[:, :])
                        tr.then_inc(x1T_done, 1)
                if k in FFN_SLOTS:
                    f = FFN_SLOTS[k]
                    if f == 0:
                        pe.wait_ge(x1T_copied, b * 2)
                    else:
                        pe.wait_ge(h_done, (b - 1) * NF + f)
                    for i, w in enumerate((wg, wu)):
                        for c in range(C):
                            mm = nc.tensor.matmul(side_ps[i][:, :], w[:, c, f * P:(f + 1) * P], x1T[:, c, :],
                                                  start=(c == 0), stop=(c == C - 1))
                    mm.then_inc(gate_done, 1)
                if k == DOWN:
                    pe.wait_ge(h_done, b * NF)
                    for i in range(2):
                        for n in range(2):
                            t = 2 * i + n
                            for f in range(NF):
                                mm = nc.tensor.matmul(side_ps[i][:, n * DM:(n + 1) * DM],
                                                      hT[:, f, t * P:(t + 1) * P], wd[:, f, :],
                                                      start=(f == 0), stop=(f == NF - 1))
                        mm.then_inc(down_done, 1)

            pe.wait_ge(consts_done, 3)
            pe.wait_ge(w_loaded, 16 * N_W + 16)
            pe.wait_ge(xT_loaded, 16)
            for G in range(3):
                for what in range(3):
                    if G + what:
                        pe.wait_ge(proj_copied, 3 * G + what)
                    project_products(G, what)
                if G == 0:
                    scores(0, 0, 0, False)
            slots(0, True, False)
            pe.wait_ge(ffn_loaded, 16 * 5)
            pe.wait_ge(deq_done, 3)
            with pe.Fori(1, B) as b:
                slots(b, False, False)
            slots(B, False, True)

        @block.vector
        def _(dve):
            def search(T0, U0, j):
                buf = top[:, j % 4, :, :]
                for r in range(4):
                    for a in range(2):
                        if r == 0:
                            wait_apart(dve, s_copied, T0 + a + 1)
                            nc.vector.max(buf[:, a, 0:8], S[:, j % 4, a, :]).then_inc(max_done, 1)
                            continue
                        dve.wait_ge(dve_step, U0 + 4 * r - 2 + a - 1)
                        mx = nc.vector.max(buf[:, a, 8 * r:8 * r + 8], W[:, a, :])
                        mx.then_inc(dve_step, 1) if r < 3 else mx.then_inc(thr_done, 1)
                    if r == 3:
                        break
                    for a in range(2):
                        if r == 0:
                            wait_apart(dve, max_done, T0 + a + 1)
                        else:
                            dve.wait_ge(dve_step, U0 + 4 * r + a - 1)
                        nc.vector.match_replace(out=W[:, a, :], in_to_replace=buf[:, a, 8 * r:8 * r + 8],
                                                in_values=(S[:, j % 4, a, :] if r == 0 else W[:, a, :]),
                                                imm_value=GONE).then_inc(dve_step, 1)

            def normalise(grp, G):
                turned = work_ps[:, :].rearrange("p (n h v) -> p n h v", n=NT, h=HG)
                dve.wait_ge(turned_done, G)
                nc.vector.reciprocal(rden[:, :, :], turned[:, :, :, D]).then_inc(rden_done, 1)
                dve.wait_ge(rden_done, G)
                nc.vector.tensor_tensor(ctxs[:, :, grp * HG:(grp + 1) * HG, :], turned[:, :, :, 0:D],
                                        rden[:, :, :].unsqueeze(3).to_broadcast([P, NT, HG, D]),
                                        ALU.mult).then_inc(ctx_taken, 1)

            def residual(b, i, ready, base):
                src = base[:, :, :]
                for h in range(2):
                    dve.wait_ge(ready, b * 2 - 1 + h)
                    nc.vector.tensor_tensor(res[:, 2 * h:2 * h + 2, :],
                                            side_ps[h][:, :].rearrange("p (n d) -> p n d", n=2),
                                            src[:, 2 * h:2 * h + 2, :], ALU.add).then_inc(res_done, 1)
                n0 = (b - 1) * 4 + 2 * i
                for t in range(NT):
                    dve.wait_ge(res_done, n0 + 1 + t // 2)
                    nc.vector.bn_stats(stats[:, t, :], res[:, t, :]).then_inc(stats_done, 1)
                for t in range(NT):
                    wait_apart(dve, stats_done, (b - 1) * 2 * NT + i * NT + t + 1)
                    nc.vector.bn_aggr(mv[:, t, :], stats[:, t, :]).then_inc(mv_done, 1)

            def slots(b, first, rest):
                if not first:
                    dve.drain()
                    dve.sem_clear(dve_step)
                for k in range(PAIRS):
                    T = b * TILES + 2 * k
                    m = k // GP
                    if not rest:
                        search(T, 10 * k, k)
                    if k % GP == CTX_SLOT and not (first and m == 0) and not (rest and m > 0):
                        normalise((m + 3) % NG, b * NG + m)
                    if first:
                        continue
                    if k == OUT_PROJ:
                        dve.wait_ge(x_loaded, b * 16)
                        residual(b, 0, oproj_done, xs)
                    if k - 1 in FFN_SLOTS:
                        n = (b - 1) * NF + FFN_SLOTS[k - 1] + 1
                        dve.wait_ge(th_done, n)
                        nc.vector.scalar_tensor_tensor(out=hgs[:, :], in0=th[:, :], scalar=1.0, in1=side_ps[0][:, :],
                                                       op0=ALU.add, op1=ALU.mult).then_inc(hg_done, 1)
                        dve.wait_ge(hg_done, n)
                        nc.vector.scalar_tensor_tensor(out=hT[:, FFN_SLOTS[k - 1], :], in0=hgs[:, :], scalar=0.5,
                                                       in1=side_ps[1][:, :], op0=ALU.mult,
                                                       op1=ALU.mult).then_inc(h_done, 1)
                    if k == DOWN:
                        residual(b, 1, down_done, x1)

            for t in (*wqk, *bqk):
                nc.vector.memset(t[:], 0.0).then_inc(pads_zero, 1)
            nc.vector.memset(ones[:, :], 1.0).then_inc(consts_done, 1)
            nc.vector.memset(V[:, :, :, D:VW], 0.0).then_inc(consts_done, 1)
            dve.wait_ge(consts_done, 2)
            nc.vector.memset(V[:, :, :, D:D + 1], 1.0).then_inc(consts_done, 1)
            slots(0, True, False)
            with dve.Fori(1, B) as b:
                slots(b, False, False)
            slots(B, False, True)

        @block.gpsimd
        def _(pool):
            def probabilities(T0, j, first, k):
                for a in range(2):
                    wait_apart(pool, thr_done, T0 + a + 1)
                    if not (first and k < 2):
                        wait_apart(pool, p_done, T0 + a - 1)
                    nc.gpsimd.tensor_scalar(keep[:, a, :], S[:, j % 4, a, :], top[:, j % 4, a, TOP - 1:TOP], None,
                                            ALU.is_ge).then_inc(keep_done, 1)
                for a in range(2):
                    pool.wait_ge(keep_done, T0 + a + 1)
                    pool.wait_ge(exp_done, T0 + a + 1)
                    if not (first and k < 3):
                        pool.wait_ge(pT_done, T0 + a - 3)
                    nc.gpsimd.tensor_tensor(Pm[:, j % 2, a, :], E[:, j % 2, a, :], keep[:, a, :],
                                            ALU.mult).then_inc(p_done, 1)

            def layer_norm(b, i, dst, done):
                n = (b - 1) * 2 + i
                wait_apart(pool, mv_done, (n + 1) * NT)
                nc.gpsimd.tensor_scalar(veps[:, :], mv[:, :, 1], EPS, None, ALU.add).then_inc(ln_step, 1)
                pool.wait_ge(ln_step, 2 * n + 1)
                nc.gpsimd.tensor_tensor(rstd[:, :], veps[:, :], minus_half[:, :], ALU.pow).then_inc(ln_step, 1)
                wait_apart(pool, ln_step, 2 * n + 2)
                for t in range(NT):
                    nc.gpsimd.tensor_scalar(dst[:, t, :], res[:, t, :], mv[:, t, 0:1], rstd[:, t:t + 1],
                                            ALU.subtract, ALU.mult).then_inc(done, 1)

            def slots(b, first, rest):
                for k in range(PAIRS):
                    T = b * TILES + 2 * k
                    if (k == 0 and not first) or (k > 0 and not rest):
                        probabilities(T - 2, (k - 1) % PAIRS, first, k)
                    if not rest:
                        for a in range(2):
                            wait_apart(pool, max_done, T + a + 1)
                            nc.gpsimd.tensor_scalar(nmax[:, k % 4, a:a + 1], top[:, k % 4, a, 0:1], -SCALE, None,
                                                    ALU.mult).then_inc(nmax_done, 1)
                    if first:
                        continue
                    if k == OUT_PROJ + 1:
                        layer_norm(b, 0, x1, x1_done)
                    if k == DOWN + 1:
                        pool.wait_ge(stored, 16 * b)
                        layer_norm(b, 1, outs, out_done)

            nc.gpsimd.memset(minus_half[:, :], -0.5)
            nc.gpsimd.memset(outs[:, :, :], 0.0).then_inc(stored, 16)
            pool.wait_ge(ffn_loaded, 16 * 5)
            for i, w in enumerate((wg, wu, wd)):
                nc.gpsimd.tensor_scalar(w[:, :, :].rearrange("p a n -> p (a n)"), wint[:, i, :], DEQ, None,
                                        ALU.mult).then_inc(deq_done, 1)
            slots(0, True, False)
            with pool.Fori(1, B) as b:
                slots(b, False, False)
            slots(B, False, True)


_INS = ["xT", "x", "wqT", "wkT", "wvT", "woT", "bq", "bk", "bv", "bo", "wgT", "wuT", "wdT", "ident"]


def kernel(L0_attn_x, L0_attn_Wq, L0_attn_bq, L0_attn_Wk, L0_attn_bk, L0_attn_Wv, L0_attn_bv, L0_attn_Wo,
           L0_attn_bo, L0_ffn_w_gate, L0_ffn_w_up, L0_ffn_w_down):
    import concourse.bacc as _bacc
    from concourse.bass_utils import run_bass_kernel_spmd as _run

    laid_out = {
        "xT": L0_attn_x.transpose(0, 2, 1), "x": L0_attn_x,
        "wqT": L0_attn_Wq.T, "wkT": L0_attn_Wk.T, "wvT": L0_attn_Wv.T, "woT": L0_attn_Wo.T,
        
        "bq": L0_attn_bq.reshape(NG, HG, D).transpose(1, 2, 0), "bk": L0_attn_bk.reshape(NG, HG, D).transpose(1, 2, 0),
        "bv": L0_attn_bv, "bo": L0_attn_bo,
        "wgT": L0_ffn_w_gate.T, "wuT": L0_ffn_w_up.T, "wdT": L0_ffn_w_down.T,
        "ident": np.eye(P, dtype=np.float32),
    }
    nc = _bacc.Bacc("TRN2", target_bir_lowering=False, num_devices=1)
    arrays, args = {}, []
    for name in _INS:
        a = np.ascontiguousarray(laid_out[name])
        arrays[f"in_{name}"] = a
        args.append(nc.dram_tensor(f"in_{name}", a.shape, mybir.dt.from_np(a.dtype), kind="ExternalInput").ap())
    out = nc.dram_tensor("out", (B, L, DM), F32, kind="ExternalOutput").ap()
    build(nc, *args, out)
    r = _run(nc, [arrays], core_ids=[0])
    return r.results[0]["out"]
```

```python
from contextlib import ExitStack

import numpy as np

import concourse.bass as bass
from concourse import mybir

B, L, DM = 16, 512, 256
H, D = 16, 16
HID = 768
TOP = 31
P = 128
C = DM // P
NT = L // P
HG = P // 32
NG = H // HG
NF = HID // P
VW = 32
PAIRS = H * NT // 2
GP = PAIRS // NG
TILES = 2 * PAIRS
SCALE = float(D) ** -0.5
DEQ = float(np.float32(1.0 / 127.0))
EPS = 1e-5
GONE = -3.0e38

Z = 1.8
ZQ = Z * 1.001
NB = 8
BW = L // NB
NC = NB * 8
RANKS = 24
LEAST = TOP - RANKS
TINY = 1.0e-30

STATS = 1
SPLIT = 2
FINISH = 3
CHECK = 4
PROB = 5
TURN = 6
PV = 7
CTX_T, OUT_PROJ, X1_T, FFN0, DOWN = 8, 9, 13, 15, 27
FFN_SLOTS = {FFN0 + 2 * f: f for f in range(NF)}
DOWN_TILES = {DOWN: (0,), DOWN + 1: (1,), DOWN + 2: (2, 3)}
CTX_SLOT = PV
PROJ_SLOTS = {0: 0, 2: 1, 4: 2}
AHEAD = 2

F32 = mybir.dt.float32
I32 = mybir.dt.int32
BF16 = mybir.dt.bfloat16
ALU = mybir.AluOpType
ACT = mybir.ActivationFunctionType


def pair_place(j):
    grp, r = divmod(j, GP)
    return grp, r // 2, 2 * (r % 2)


def due(lag, k, first, rest):
    return (k >= lag and not rest) or (k < lag and not first)


def build(nc, xT, x, wqT, wkT, wvT, woT, bq, bk, bv, bo, wgT, wuT, wdT, ident_in, ranks_in, out):
    with ExitStack() as ctx:
        def sb(name, shape, dt=F32):
            return ctx.enter_context(nc.sbuf_tensor(name, shape, dt))

        def ps(name, shape):
            return ctx.enter_context(nc.psum_tensor(name, shape, F32))

        def sem(name):
            return ctx.enter_context(nc.semaphore(name))

        ident = sb("ident", [P, P])
        ones = sb("ones", [1, P])
        wqk = [sb(f"w{n}", [P, C, NG, HG, 32]) for n in "qk"]
        bqk = [sb(f"b{n}", [P, NG]) for n in "qk"]
        wv = sb("wv", [P, C, DM])
        wo = sb("wo", [P, C, DM])
        bvc = sb("bvc", [P, C])
        brow = sb("brow", [1, DM])
        wint = sb("wint", [P, 3, C * HID], I32)
        wg = sb("wg", [P, C, HID])
        wu = sb("wu", [P, C, HID])
        wd = sb("wd", [P, NF, DM])
        minus_half = sb("minus_half", [P, NT])
        half = sb("half", [P, 2])

        xTs = sb("xTs", [P, C, L])
        xs = sb("xs", [P, NT, DM])
        QKT = [sb(f"{n}T", [P, NG, L]) for n in "QK"]
        V = sb("V", [P, NT, H, VW])
        ctxs = sb("ctxs", [P, NT, H, D])
        ctxr = sb("ctxr", [P, L])
        rden = sb("rden", [P, NT, HG])
        ctxT = sb("ctxT", [P, C, L])
        res = sb("res", [P, NT, DM])
        stats = sb("stats", [P, NT, 6])
        mv = sb("mv", [P, NT, 2])
        veps = sb("veps", [P, NT])
        rstd = sb("rstd", [P, NT])
        mrstd = sb("mrstd", [P, NT])
        shift = sb("shift", [P, NT])
        x1 = sb("x1", [P, NT, DM])
        x1T = sb("x1T", [P, C, L])
        th = sb("th", [P, L])
        ups = sb("ups", [P, L])
        hgs = sb("hgs", [P, L])
        hT = sb("hT", [P, NF, L])
        outs = sb("outs", [P, NT, DM])

        S = sb("S", [P, 8, 2, L])
        W = sb("W", [P, L])
        Y = sb("Y", [P, 2, L])
        junk = sb("junk", [P, 4, L], BF16)
        ssum = sb("ssum", [P, 4, 2])
        ssq = sb("ssq", [P, 4, 2])
        msq = sb("msq", [P, 2, 2])
        zvar = sb("zvar", [P, 2, 2])
        zsd = sb("zsd", [P, 8, 2])
        cnt = sb("cnt", [P, 4, 2])
        mean = sb("mean", [P, 2, 2])
        guess = sb("guess", [P, 4, 2])
        top = sb("top", [P, 8, 2, 8])
        cand = sb("cand", [P, 2, 2, NB, 8])
        left = sb("left", [P, 2, NC])
        best = sb("best", [P, 2, RANKS])
        hit = sb("hit", [P, 2, RANKS])
        counts = sb("counts", [P, RANKS])
        hidden = sb("hidden", [P, 2])
        flag = sb("flag", [P, 2, 2])
        flag_i = sb("flag_i", [1, 2, 4], I32)
        onesc = sb("onesc", [P, 1])
        thr = sb("thr", [P, 8, 2])
        gtop = sb("gtop", [P, 3, 8])
        nmax = sb("nmax", [P, 8, 2])
        E = sb("E", [P, 4, 2, L])
        keep = sb("keep", [P, 2, L])
        Pm = sb("Pm", [P, 2, 2, L])
        PT = sb("PT", [P, 2, 2, L])

        S_ps = [ps(f"S_ps{a}", [P, L]) for a in range(2)]
        PT_ps = [ps(f"PT_ps{a}", [P, L]) for a in range(2)]
        ctxT_ps = ps("ctxT_ps", [P, L])
        side_ps = [ps(f"side_ps{a}", [P, L]) for a in range(2)]
        work_ps = ps("work_ps", [P, L])

        w_loaded = sem("w_loaded")
        ffn_loaded = sem("ffn_loaded")
        xT_loaded = sem("xT_loaded")
        x_loaded = sem("x_loaded")
        pads_zero = sem("pads_zero")
        consts_done = sem("consts_done")
        deq_done = sem("deq_done")
        proj_done = sem("proj_done")
        proj_copied = sem("proj_copied")
        scores_done = sem("scores_done")
        s_copied = sem("s_copied")
        max_done = sem("max_done")
        dve_step = sem("dve_step")
        general_step = sem("general_step")
        sq_done = sem("sq_done")
        var_done = sem("var_done")
        half_set = sem("half_set")
        sd_step = sem("sd_step")
        guess_done = sem("guess_done")
        cnt_done = sem("cnt_done")
        flag_done = sem("flag_done")
        flag_summed = sem("flag_summed")
        flag_copied = sem("flag_copied")
        thr_done = sem("thr_done")
        nmax_done = sem("nmax_done")
        exp_done = sem("exp_done")
        keep_done = sem("keep_done")
        p_done = sem("p_done")
        pT_done = sem("pT_done")
        pT_copied = sem("pT_copied")
        pv_done = sem("pv_done")
        raw_copied = sem("raw_copied")
        turned_done = sem("turned_done")
        rden_done = sem("rden_done")
        ctx_taken = sem("ctx_taken")
        ctxT_done = sem("ctxT_done")
        ctxT_copied = sem("ctxT_copied")
        brow_done = sem("brow_done")
        brow_copied = sem("brow_copied")
        oproj_done = sem("oproj_done")
        res_done = sem("res_done")
        stats_done = sem("stats_done")
        mv_done = sem("mv_done")
        ln_step = sem("ln_step")
        mrstd_done = sem("mrstd_done")
        x1_done = sem("x1_done")
        x1T_done = sem("x1T_done")
        x1T_copied = sem("x1T_copied")
        gate_done = sem("gate_done")
        th_done = sem("th_done")
        up_copied = sem("up_copied")
        hg_done = sem("hg_done")
        h_done = sem("h_done")
        down_done = sem("down_done")
        out_done = sem("out_done")
        stored = sem("stored")

        N_W = 15
        block = ctx.enter_context(nc.Block())

        def wait_apart(eng, s, value):
            eng.wait_ge(s, value)
            eng.nop(nofuse=True)


        @block.sync
        def _(sp):
            def load_xT(b):
                sp.dma_start(xTs[:, :, :], xT[b].rearrange("(c p) t -> p c t", p=P)).then_inc(xT_loaded, 16)

            def load_x(b):
                sp.dma_start(xs[:, :, :], x[b].rearrange("(n p) d -> p n d", p=P)).then_inc(x_loaded, 16)

            def store(b):
                sp.dma_start(out[b].rearrange("(n p) d -> p n d", p=P), outs[:, :, :]).then_inc(stored, 16)

            load_xT(0)
            sp.dma_start(counts[:, :], ranks_in).then_inc(w_loaded, 16)
            sp.wait_ge(pads_zero, 4)
            for w, src in ((0, wqT), (1, wkT)):
                for c in range(C):
                    sp.dma_start(wqk[w][:, c, :, :, 0:D],
                                 src[c * P:(c + 1) * P, :].rearrange("p (g s d) -> p g s d", g=NG, s=HG)
                                 ).then_inc(w_loaded, 16)
            for w, src in ((0, bq), (1, bk)):
                for i in range(HG):
                    sp.dma_start(bqk[w][32 * i:32 * i + D, :],
                                 src[i]).then_inc(w_loaded, 16)
            sp.dma_start(wv[:, :, :], wvT.rearrange("(c p) n -> p c n", p=P)).then_inc(w_loaded, 16)
            sp.dma_start(bvc[:, :], bv).then_inc(w_loaded, 16)
            load_x(0)

            def steps(b, last):
                sp.wait_ge(proj_done, b * 12 + 12)
                load_xT(b if last else b + 1)
                sp.wait_ge(res_done, b * 4 - 2)
                load_x(b)
                sp.wait_ge(out_done, b * NT)
                store(b - 1)

            sp.wait_ge(proj_done, 12)
            load_xT(1)
            with sp.Fori(1, B - 1) as b:
                steps(b, False)
            steps(B - 1, True)
            sp.wait_ge(out_done, B * NT)
            store(B - 1)
            sp.wait_ge(stored, 16 * (B + 1))
            sp.wait_ge(xT_loaded, 16 * (B + 1))

        @block.scalar
        def _(act):
            act.dma_start(ident[:, :], ident_in).then_inc(w_loaded, 16)
            act.dma_start(wo[:, :, :], woT.rearrange("(c p) n -> p c n", p=P)).then_inc(ffn_loaded, 16)
            act.dma_start(brow[:, :], bo.rearrange("(a n) -> a n", a=1)).then_inc(ffn_loaded, 16)
            for i, w in enumerate((wgT, wuT, wdT)):
                act.dma_start(wint[:, i, :].rearrange("p (c n) -> p c n", n=w.shape[1]),
                              w.rearrange("(c p) n -> p c n", p=P)).then_inc(ffn_loaded, 16)

            def project_copy(G, grp, what):
                act.wait_ge(proj_done, 3 * G + what + 1)
                if what < 2:
                    nc.scalar.activation(QKT[what][:, grp, :], work_ps[:, :], ACT.Identity,
                                         bias=bqk[what][:, grp:grp + 1]).then_inc(proj_copied, 1)
                else:
                    nc.scalar.activation(V[:, :, grp * HG:(grp + 1) * HG, 0:D],
                                         work_ps[:, 0:NT * HG * D].rearrange("p (n h d) -> p n h d", n=NT, h=HG),
                                         ACT.Copy).then_inc(proj_copied, 1)

            def copy_scores(T, n, k, first):
                for a in range(2):
                    act.wait_ge(scores_done, T + a + 1)
                    if not (first and k < 8):
                        act.wait_ge(p_done, T + a - 15)
                    if not (first and k < 4):
                        act.wait_ge(var_done, n - 3)
                    nc.scalar.activation(S[:, k % 8, a, :], S_ps[a][:, :], ACT.Copy,
                                         accum_out=ssum[:, k % 4, a:a + 1]).then_inc(s_copied, 1)

            def sum_squares(T, k, first):
                for a in range(2):
                    act.wait_ge(s_copied, T + a + 1)
                    if not (first and k < 1):
                        act.wait_ge(sq_done, T + a - 1)
                    nc.scalar.activation(junk[:, a, :], S[:, k % 8, a, :], ACT.Square,
                                         scale=ZQ / float(np.sqrt(L)), accum_out=ssq[:, k % 4, a:a + 1]).then_inc(sq_done, 1)

            def count_below(T0, n, j, first, k):
                for a in range(2):
                    act.wait_ge(guess_done, n + 1)
                    if not (first and k < SPLIT + 1):
                        act.wait_ge(cnt_done, T0 + a - 1)
                    if not (first and k < SPLIT + 4):
                        act.wait_ge(flag_done, n - 3)
                    nc.scalar.activation(junk[:, 2 + a, :], S[:, j % 8, a, :], ACT.Sign,
                                         bias=guess[:, j % 4, a:a + 1], scale=-1.0,
                                         accum_out=cnt[:, j % 4, a:a + 1]).then_inc(cnt_done, 1)

            def exponentials(T0, n, j, first, k):
                for a in range(2):
                    act.wait_ge(nmax_done, n + 1)
                    if not (first and k < SPLIT + 4):
                        act.wait_ge(p_done, T0 + a - 7)
                    nc.scalar.activation(E[:, j % 4, a, :], S[:, j % 8, a, :], ACT.Exp,
                                         bias=nmax[:, j % 8, a:a + 1], scale=SCALE).then_inc(exp_done, 1)

            def normalised(b, i, dst, done):
                act.wait_ge(mrstd_done, (b - 1) * 4 + 2 * i + 2)
                for t in range(NT):
                    nc.scalar.activation(dst[:, t, :], res[:, t, :], ACT.Identity, bias=shift[:, t:t + 1],
                                         scale=rstd[:, t:t + 1]).then_inc(done, 1)

            def slots(b, first, rest):
                for k in range(PAIRS):
                    T = b * TILES + 2 * k
                    n = b * PAIRS + k
                    if k % GP == CTX_SLOT and not (first and k < GP) and not (rest and k >= GP):
                        act.wait_ge(pv_done, b * PAIRS + k - CTX_SLOT)
                        nc.scalar.activation(ctxr[:, :], ctxT_ps[:, :], ACT.Copy).then_inc(raw_copied, 1)
                    if not first and k - 1 in FFN_SLOTS:
                        n_f = (b - 1) * NF + FFN_SLOTS[k - 1]
                        act.wait_ge(gate_done, n_f + 1)
                        nc.scalar.activation(th[:, :], side_ps[0][:, :], ACT.Tanh, scale=0.5).then_inc(th_done, 1)
                        if FFN_SLOTS[k - 1]:
                            act.wait_ge(h_done, n_f)
                        nc.scalar.activation(ups[:, :], side_ps[1][:, :], ACT.Copy, scale=0.5).then_inc(up_copied, 1)
                    if not rest:
                        copy_scores(T, n, k, first)
                    if due(CHECK, k, first, rest):
                        act.wait_ge(flag_summed, n - CHECK + 1)
                        if not (first and k < CHECK + 2):
                            act.wait_ge(thr_done, n - CHECK - 1)
                        nc.scalar.activation(flag_i[0:1, (k - CHECK) % 2, 0:3], work_ps[0:1, 0:3],
                                             ACT.Copy).then_inc(flag_copied, 1)
                    if not rest:
                        sum_squares(T, k, first)
                    if due(SPLIT, k, first, rest):
                        exponentials(T - 2 * SPLIT, n - SPLIT, (k - SPLIT) % PAIRS, first, k)
                    if due(TURN, k, first, rest):
                        for a in range(2):
                            act.wait_ge(pT_done, T - 2 * TURN + a + 1)
                            if not (first and k < TURN + 2):
                                act.wait_ge(pv_done, b * PAIRS + k - TURN - 1)
                            nc.scalar.activation(PT[:, (k - TURN) % 2, a, :], PT_ps[a][:, :],
                                                 ACT.Copy).then_inc(pT_copied, 1)
                    if due(SPLIT, k, first, rest):
                        count_below(T - 2 * SPLIT, n - SPLIT, (k - SPLIT) % PAIRS, first, k)
                    if not rest and k % GP in PROJ_SLOTS:
                        m = k // GP + AHEAD
                        project_copy(b * NG + m, m % NG, PROJ_SLOTS[k % GP])
                    if first:
                        continue
                    if k == OUT_PROJ + 3:
                        normalised(b, 0, x1, x1_done)
                    if k == DOWN + 4:
                        act.wait_ge(stored, 16 * b)
                        normalised(b, 1, outs, out_done)
                    if k == CTX_T:
                        for i in range(2):
                            act.wait_ge(ctxT_done, b * 2 - 1 + i)
                            nc.scalar.activation(ctxT[:, :, i * 2 * P:(i + 1) * 2 * P]
                                                 .rearrange("p c (n t) -> p n c t", n=2),
                                                 side_ps[i][:, :].rearrange("p (n c t) -> p n c t", n=2, c=C),
                                                 ACT.Copy).then_inc(ctxT_copied, 1)
                    if k == X1_T:
                        for i in range(2):
                            act.wait_ge(x1T_done, b * 2 - 1 + i)
                            nc.scalar.activation(x1T[:, :, i * 2 * P:(i + 1) * 2 * P]
                                                 .rearrange("p c (n t) -> p n c t", n=2),
                                                 side_ps[i][:, :].rearrange("p (n c t) -> p n c t", n=2, c=C),
                                                 ACT.Copy).then_inc(x1T_copied, 1)

            act.wait_ge(consts_done, 3)
            act.wait_ge(w_loaded, 16 * N_W + 16)
            for G in range(AHEAD):
                for what in range(3):
                    project_copy(G, G, what)
            slots(0, True, False)
            act.wait_ge(brow_done, 1)
            nc.scalar.activation(brow[:, :], side_ps[0][0:1, 0:DM], ACT.Copy).then_inc(brow_copied, 1)
            with act.Fori(1, B) as b:
                slots(b, False, False)
            slots(B, False, True)

        @block.tensor
        def _(pe):
            def project_products(grp, what):
                if what < 2:
                    for c in range(C):
                        mm = nc.tensor.matmul(work_ps[:, :], wqk[what][:, c, grp, :, :].rearrange("p s d -> p (s d)"),
                                              xTs[:, c, :], start=(c == 0), stop=(c == C - 1))
                else:
                    n = HG * D
                    for t in range(NT):
                        o = work_ps[:, t * n:(t + 1) * n]
                        for c in range(C):
                            mm = nc.tensor.matmul(o, xTs[:, c, t * P:(t + 1) * P], wv[:, c, grp * n:(grp + 1) * n],
                                                  start=(c == 0), stop=(c == C - 1))
                mm.then_inc(proj_done, 1)

            def scores(T, G, k, first):
                grp, strip, q0 = pair_place(k)
                if k % GP == 0:
                    pe.wait_ge(proj_copied, 3 * G + 2)
                for a in range(2):
                    if not (first and k == 0):
                        pe.wait_ge(s_copied, T + a - 1)
                    lo = 32 * strip
                    q = (q0 + a) * P
                    nc.tensor.matmul(S_ps[a][:, :], QKT[0][lo:lo + D, grp, q:q + P], QKT[1][lo:lo + D, grp, :],
                                     start=True, stop=True, tile_position=(lo, 0)).then_inc(scores_done, 1)

            def sum_flags(b, k, first, rest):
                pe.wait_ge(flag_done, b * PAIRS + k - CHECK + 1)
                m, r = divmod(k, GP)
                projected = 0 if rest else 3 * m + sum(r > slot for slot in PROJ_SLOTS)
                pe.wait_ge(proj_copied, 3 * (b * NG + AHEAD) + projected)
                turned = m - 1
                if not (first and m < 2):
                    pe.wait_ge(ctx_taken, b * NG + turned)
                if not (first and k == CHECK):
                    pe.wait_ge(flag_copied, b * PAIRS + k - CHECK)
                c = (k - CHECK) % 2
                nc.tensor.matmul(work_ps[0:1, 0:2], onesc[:, :], flag[:, c, :], start=True, stop=True)
                for a in range(2):
                    mm = nc.tensor.matmul(work_ps[0:1, 2:3], onesc[:, :], flag[:, c, a:a + 1],
                                          start=(a == 0), stop=(a == 1))
                mm.then_inc(flag_summed, 1)

            def turn(T0, j, a, first, k):
                pe.wait_ge(p_done, T0 + a + 1)
                if not (first and k == TURN):
                    pe.wait_ge(pT_copied, T0 + a - 1)
                for i in range(NT):
                    tr = nc.tensor.transpose(PT_ps[a][:, i * P:(i + 1) * P],
                                             Pm[:, j % 2, a, i * P:(i + 1) * P], ident[:, :])
                tr.then_inc(pT_done, 1)

            def values(T0, G, j, first_group):
                grp, strip, q0 = pair_place(j)
                if j % GP == 0:
                    pe.wait_ge(proj_copied, 3 * G + 3)
                    if not first_group:
                        pe.wait_ge(raw_copied, G)
                pe.wait_ge(pT_copied, T0 + 2)
                for n in range(NT):
                    mm = nc.tensor.matmul(ctxT_ps[32 * strip:32 * strip + VW, q0 * P:(q0 + 2) * P],
                                          V[:, n, grp * HG + strip, :], PT[:, j % 2, :, n * P:(n + 1) * P],
                                          start=(n == 0), stop=(n == NT - 1), tile_position=(0, 32 * strip))
                mm.then_inc(pv_done, 1)

            def turn_context(G, flags_out, rest):
                pe.wait_ge(raw_copied, G)
                pe.wait_ge(proj_copied, 3 * (G + AHEAD + 1) if not rest else 3 * (G + AHEAD))
                pe.wait_ge(flag_copied, flags_out)
                for n in range(NT):
                    tr = nc.tensor.transpose(work_ps[:, n * P:(n + 1) * P], ctxr[:, n * P:(n + 1) * P], ident[:, :])
                tr.then_inc(turned_done, 1)

            def slots(b, first, rest):
                for k in range(PAIRS):
                    T = b * TILES + 2 * k
                    n = b * PAIRS + k
                    if not rest:
                        scores(T, b * NG + k // GP, k, first)
                    flags_out = b * PAIRS if rest and k >= CHECK else n - CHECK + 1
                    if due(CHECK, k, first, rest):
                        sum_flags(b, k, first, rest)
                    for a in range(2):
                        if due(TURN, k, first, rest):
                            turn(T - 2 * TURN, (k - TURN) % PAIRS, a, first, k)
                    if due(PV, k, first, rest):
                        values(T - 2 * PV, b * NG + (k - PV) // GP, (k - PV) % PAIRS, first and k == PV)
                    if k % GP == CTX_SLOT and not (first and k < GP) and not (rest and k >= GP):
                        turn_context(b * NG + k // GP, flags_out, rest)
                    if not rest and k % GP in PROJ_SLOTS:
                        m, what = k // GP, PROJ_SLOTS[k % GP]
                        if what == 0:
                            if not (first and m < 2):
                                pe.wait_ge(ctx_taken, b * NG + m - 1)
                            pe.wait_ge(xT_loaded, (b + 1 + (m + AHEAD >= NG)) * 16)
                        if not (first and k < CHECK):
                            pe.wait_ge(flag_copied, flags_out)
                        pe.wait_ge(proj_copied, (b * NG + m + AHEAD) * 3 + what)
                        project_products((m + AHEAD) % NG, what)
                    if not first:
                        tail(b, k)

            def tail(b, k):
                if k == CTX_T:
                    pe.wait_ge(ctx_taken, b * NG)
                    for i in range(2):
                        for n in range(2):
                            for c in range(C):
                                tr = nc.tensor.transpose(
                                    side_ps[i][:, (n * C + c) * P:(n * C + c + 1) * P],
                                    ctxs[:, 2 * i + n, c * P // D:(c + 1) * P // D, :].rearrange("p h d -> p (h d)"),
                                    ident[:, :])
                        tr.then_inc(ctxT_done, 1)
                if k == OUT_PROJ:
                    for i in range(2):
                        pe.wait_ge(ctxT_copied, b * 2 - 1 + i)
                        for n in range(2):
                            t = 2 * i + n
                            o = side_ps[i][:, n * DM:(n + 1) * DM]
                            for c in range(C):
                                nc.tensor.matmul(o, ctxT[:, c, t * P:(t + 1) * P], wo[:, c, :],
                                                 start=(c == 0), stop=False)
                            mm = nc.tensor.matmul(o, ones[:, :], brow[:, :], start=False, stop=True)
                        mm.then_inc(oproj_done, 1)
                if k == X1_T:
                    pe.wait_ge(x1_done, b * NT)
                    for i in range(2):
                        for n in range(2):
                            for c in range(C):
                                tr = nc.tensor.transpose(side_ps[i][:, (n * C + c) * P:(n * C + c + 1) * P],
                                                         x1[:, 2 * i + n, c * P:(c + 1) * P], ident[:, :])
                        tr.then_inc(x1T_done, 1)
                if k in FFN_SLOTS:
                    f = FFN_SLOTS[k]
                    if f == 0:
                        pe.wait_ge(x1T_copied, b * 2)
                    else:
                        pe.wait_ge(hg_done, (b - 1) * NF + f)
                        pe.wait_ge(up_copied, (b - 1) * NF + f)
                    for i, w in enumerate((wg, wu)):
                        for c in range(C):
                            mm = nc.tensor.matmul(side_ps[i][:, :], w[:, c, f * P:(f + 1) * P], x1T[:, c, :],
                                                  start=(c == 0), stop=(c == C - 1))
                    mm.then_inc(gate_done, 1)
                if k in DOWN_TILES:
                    pe.wait_ge(h_done, b * NF)
                    for t in DOWN_TILES[k]:
                        for f in range(NF):
                            mm = nc.tensor.matmul(side_ps[t // 2][:, t % 2 * DM:(t % 2 + 1) * DM],
                                                  hT[:, f, t * P:(t + 1) * P], wd[:, f, :],
                                                  start=(f == 0), stop=(f == NF - 1))
                        if t % 2:
                            mm.then_inc(down_done, 1)

            pe.wait_ge(consts_done, 3)
            pe.wait_ge(w_loaded, 16 * N_W + 16)
            pe.wait_ge(xT_loaded, 16)
            for G in range(AHEAD):
                for what in range(3):
                    if G + what:
                        pe.wait_ge(proj_copied, 3 * G + what)
                    project_products(G, what)
            slots(0, True, False)
            pe.wait_ge(ffn_loaded, 16 * 5)
            for c in range(C):
                nc.tensor.matmul(side_ps[0][0:1, 0:DM], bvc[:, c:c + 1], wo[:, c, :], start=(c == 0), stop=False)
            nc.tensor.matmul(side_ps[0][0:1, 0:DM], ones[:, 0:1], brow[:, :],
                             start=False, stop=True).then_inc(brow_done, 1)
            pe.wait_ge(brow_copied, 1)
            pe.wait_ge(deq_done, 3)
            with pe.Fori(1, B) as b:
                slots(b, False, False)
            slots(B, False, True)

        @block.vector
        def _(dve):
            steps = [0]

            def mark(ins):
                ins.then_inc(dve_step, 1)
                steps[0] += 1
                return steps[0]

            def row_max(T, k, a):
                wait_apart(dve, s_copied, T + a + 1)
                nc.vector.max(top[:, k % 8, a, :], S[:, k % 8, a, :]).then_inc(max_done, 1)

            def statistics(T, n, j, step):
                if step == 0:
                    dve.wait_ge(sq_done, T + 2)
                    mark(nc.vector.tensor_scalar(mean[:, j % 2, :], ssum[:, j % 4, :], 1.0 / L, None, ALU.mult))
                    statistics.msq = mark(nc.vector.scalar_tensor_tensor(
                        out=msq[:, j % 2, :], in0=ssum[:, j % 4, :], scalar=-(Z / L) ** 2, in1=ssum[:, j % 4, :],
                        op0=ALU.mult, op1=ALU.mult))
                if step == 1:
                    dve.wait_ge(dve_step, statistics.msq)
                    nc.vector.tensor_tensor(zvar[:, j % 2, :], ssq[:, j % 4, :], msq[:, j % 2, :],
                                            ALU.add).then_inc(var_done, 1)

            y_written, cand_written = [0, 0], [0, 0]

            def below(T0, n, j, a, first, k):
                dve.wait_ge(guess_done, n + 1)
                if cand_written[a]:
                    dve.wait_ge(dve_step, cand_written[a])
                y_written[a] = mark(nc.vector.scalar_tensor_tensor(
                    out=Y[:, a, :], in0=S[:, j % 8, a, :], scalar=guess[:, j % 4, a:a + 1], in1=S[:, j % 8, a, :],
                    op0=ALU.is_lt, op1=ALU.mult))

            def candidates(j, a):
                for g in range(NB):
                    dve.wait_ge(dve_step, y_written[a])
                    mx = nc.vector.max(cand[:, j % 2, a, g, :], Y[:, a, g * BW:(g + 1) * BW])
                cand_written[a] = mark(mx)

            def finish(T0, j, cands, between):
                c, sorted_to = j % 2, list(cands)
                for r in range(3):
                    for a in range(2):
                        src = cand[:, c, a, :, :].rearrange("p g e -> p (g e)") if r == 0 else left[:, a, :]
                        if sorted_to[a]:
                            dve.wait_ge(dve_step, sorted_to[a])
                        sorted_to[a] = mark(nc.vector.max(best[:, a, 8 * r:8 * r + 8], src))
                    between()
                    for a in range(2 if r < 2 else 0):
                        src = cand[:, c, a, :, :].rearrange("p g e -> p (g e)") if r == 0 else left[:, a, :]
                        dve.wait_ge(dve_step, sorted_to[a])
                        sorted_to[a] = mark(nc.vector.match_replace(
                            out=left[:, a, :], in_to_replace=best[:, a, 8 * r:8 * r + 8], in_values=src,
                            imm_value=GONE))
                    if r < 2:
                        between()
                h = mark(nc.vector.tensor_reduce(hidden[:, :], cand[:, c, :, :, 7], mybir.AxisListType.X, ALU.max))
                for a in range(2):
                    dve.wait_ge(cnt_done, T0 + a + 1)
                    dve.wait_ge(dve_step, sorted_to[a])
                    sorted_to[a] = mark(nc.vector.scalar_tensor_tensor(
                        out=hit[:, a, :], in0=counts[:, :], scalar=cnt[:, j % 4, a:a + 1], in1=best[:, a, :],
                        op0=ALU.is_equal, op1=ALU.mult, accum_out=thr[:, j % 8, a:a + 1]))
                between()
                dve.wait_ge(dve_step, max(sorted_to[1], h))
                nc.vector.scalar_tensor_tensor(out=flag[:, c, :], in0=hidden[:, :], scalar=TINY, in1=thr[:, j % 8, :],
                                               op0=ALU.max, op1=ALU.is_gt).then_inc(flag_done, 1)

            def general(j, a):
                dve.sem_clear(general_step)
                n = 0
                largest = top[:, j % 8, a, :]
                for r in range(3):
                    nc.vector.match_replace(out=W[:, :], in_to_replace=largest,
                                            in_values=S[:, j % 8, a, :] if r == 0 else W[:, :],
                                            imm_value=GONE).then_inc(general_step, 1)
                    n += 1
                    dve.wait_ge(general_step, n)
                    largest = gtop[:, r, :]
                    nc.vector.max(largest, W[:, :]).then_inc(general_step, 1)
                    n += 1
                    dve.wait_ge(general_step, n)
                nc.vector.tensor_copy(thr[:, j % 8, a:a + 1], gtop[:, 2, TOP - 25:TOP - 24]).then_inc(general_step, 1)
                dve.wait_ge(general_step, n + 1)

            def check(n, j):
                wait_apart(dve, flag_copied, n + 1)
                either = dve.value_load(flag_i[0:1, j % 2, 2:3], min_val=0, max_val=2 * P)
                with dve.If(either > 0):
                    for a in range(2):
                        flagged = dve.value_load(flag_i[0:1, j % 2, a:a + 1], min_val=0, max_val=P)
                        with dve.If(flagged > 0):
                            general(j, a)
                dve.nop(nofuse=True).then_inc(thr_done, 1)

            def normalise(grp, G):
                turned = work_ps[:, :].rearrange("p (n h v) -> p n h v", n=NT, h=HG)
                dve.wait_ge(turned_done, G)
                nc.vector.reciprocal(rden[:, :, :], turned[:, :, :, D]).then_inc(rden_done, 1)
                dve.wait_ge(rden_done, G)
                nc.vector.tensor_tensor(ctxs[:, :, grp * HG:(grp + 1) * HG, :], turned[:, :, :, 0:D],
                                        rden[:, :, :].unsqueeze(3).to_broadcast([P, NT, HG, D]),
                                        ALU.mult).then_inc(ctx_taken, 1)

            def residual(b, i, ready, base):
                src = base[:, :, :]
                for h in range(2):
                    dve.wait_ge(ready, b * 2 - 1 + h)
                    nc.vector.tensor_tensor(res[:, 2 * h:2 * h + 2, :],
                                            side_ps[h][:, :].rearrange("p (n d) -> p n d", n=2),
                                            src[:, 2 * h:2 * h + 2, :], ALU.add).then_inc(res_done, 1)
                n0 = (b - 1) * 4 + 2 * i
                for t in range(NT):
                    dve.wait_ge(res_done, n0 + 1 + t // 2)
                    nc.vector.bn_stats(stats[:, t, :], res[:, t, :]).then_inc(stats_done, 1)
                for t in range(NT):
                    wait_apart(dve, stats_done, (b - 1) * 2 * NT + i * NT + t + 1)
                    nc.vector.bn_aggr(mv[:, t, :], stats[:, t, :]).then_inc(mv_done, 1)

            def slots(b, first, rest):
                if not first:
                    dve.drain()
                    dve.sem_clear(dve_step)
                steps[0] = 0
                y_written[:] = cand_written[:] = [0, 0]
                for k in range(PAIRS):
                    T = b * TILES + 2 * k
                    n = b * PAIRS + k
                    m = k // GP
                    if k % GP == 0 and not (first and m < 2) and not (rest and m > 1):
                        normalise((m + 2) % NG, b * NG + m - 1)
                    cands = list(cand_written)
                    split_pair = (T - 2 * SPLIT, n - SPLIT, (k - SPLIT) % PAIRS)
                    split_due = due(SPLIT, k, first, rest)
                    stats_pair = (T - 2 * STATS, n - STATS, (k - STATS) % PAIRS)
                    stats_due = due(STATS, k, first, rest)

                    def long_step(i):
                        if i < 2 and stats_due:
                            row_max(stats_pair[0], stats_pair[2], i)
                        if 1 <= i < 3 and stats_due:
                            statistics(*stats_pair, i - 1)
                        if 2 <= i < 4 and split_due:
                            below(*split_pair, i - 2, first, k)
                        if 4 <= i and split_due:
                            candidates(split_pair[2], i - 4)

                    at = [0]

                    def between():
                        long_step(at[0])
                        at[0] += 1

                    if due(FINISH, k, first, rest):
                        finish(T - 2 * FINISH, (k - FINISH) % PAIRS, cands, between)
                    else:
                        for i in range(6):
                            between()
                    if due(CHECK, k, first, rest):
                        check(n - CHECK, (k - CHECK) % PAIRS)
                    if first:
                        continue
                    if k == OUT_PROJ + 1:
                        dve.wait_ge(x_loaded, b * 16)
                        residual(b, 0, oproj_done, xs)
                    if k - 1 in FFN_SLOTS:
                        n = (b - 1) * NF + FFN_SLOTS[k - 1] + 1
                        dve.wait_ge(th_done, n)
                        if FFN_SLOTS[k - 1]:
                            dve.wait_ge(h_done, n - 1)
                        nc.vector.scalar_tensor_tensor(out=hgs[:, :], in0=th[:, :], scalar=1.0, in1=side_ps[0][:, :],
                                                       op0=ALU.add, op1=ALU.mult).then_inc(hg_done, 1)
                    if k == DOWN + 3:
                        residual(b, 1, down_done, x1)

            for t in (*wqk, *bqk):
                nc.vector.memset(t[:], 0.0).then_inc(pads_zero, 1)
            nc.vector.memset(onesc[:, :], 1.0)
            nc.vector.memset(ones[:, :], 1.0).then_inc(consts_done, 1)
            nc.vector.memset(V[:, :, :, D:VW], 0.0).then_inc(consts_done, 1)
            dve.wait_ge(consts_done, 2)
            nc.vector.memset(V[:, :, :, D:D + 1], 1.0).then_inc(consts_done, 1)
            slots(0, True, False)
            with dve.Fori(1, B) as b:
                slots(b, False, False)
            slots(B, False, True)

        @block.gpsimd
        def _(pool):
            def keep_top(T0, n, j, first, k):
                for a in range(2):
                    wait_apart(pool, thr_done, n + 1)
                    if not (first and k == PROB):
                        wait_apart(pool, p_done, T0 + a - 1)
                    nc.gpsimd.tensor_scalar(keep[:, a, :], S[:, j % 8, a, :], thr[:, j % 8, a:a + 1], None,
                                            ALU.is_ge).then_inc(keep_done, 1)

            def probabilities(T0, j, first, k):
                for a in range(2):
                    pool.wait_ge(keep_done, T0 + a + 1)
                    pool.wait_ge(exp_done, T0 + a + 1)
                    if not (first and k < PROB + 2):
                        pool.wait_ge(pT_done, T0 + a - 3)
                    nc.gpsimd.tensor_tensor(Pm[:, j % 2, a, :], E[:, j % 4, a, :], keep[:, a, :],
                                            ALU.mult).then_inc(p_done, 1)

            def guess_threshold(n, j):
                pool.wait_ge(var_done, n + 1)
                nc.gpsimd.tensor_tensor(zsd[:, j % 8, :], zvar[:, j % 2, :], half[:, :], ALU.pow).then_inc(sd_step, 1)
                pool.wait_ge(sd_step, n + 1)
                nc.gpsimd.tensor_tensor(guess[:, j % 4, :], zsd[:, j % 8, :], mean[:, j % 2, :],
                                        ALU.add).then_inc(guess_done, 1)

            def layer_norm(b, i):
                n = (b - 1) * 2 + i
                wait_apart(pool, mv_done, (n + 1) * NT)
                nc.gpsimd.tensor_scalar(veps[:, :], mv[:, :, 1], EPS, None, ALU.add).then_inc(ln_step, 1)
                pool.wait_ge(ln_step, 2 * n + 1)
                nc.gpsimd.tensor_tensor(rstd[:, :], veps[:, :], minus_half[:, :], ALU.pow).then_inc(ln_step, 1)
                wait_apart(pool, ln_step, 2 * n + 2)
                nc.gpsimd.tensor_tensor(mrstd[:, :], mv[:, :, 0], rstd[:, :], ALU.mult).then_inc(mrstd_done, 1)
                wait_apart(pool, mrstd_done, 2 * n + 1)
                nc.gpsimd.tensor_scalar(shift[:, :], mrstd[:, :], -1.0, None, ALU.mult).then_inc(mrstd_done, 1)

            def slots(b, first, rest):
                for k in range(PAIRS):
                    T = b * TILES + 2 * k
                    if due(PROB, k, first, rest):
                        keep_top(T - 2 * PROB, b * PAIRS + k - PROB, (k - PROB) % PAIRS, first, k)
                    if due(STATS, k, first, rest):
                        guess_threshold(b * PAIRS + k - STATS, (k - STATS) % PAIRS)
                        j = (k - STATS) % PAIRS
                        wait_apart(pool, max_done, T - 2 * STATS + 2)
                        nc.gpsimd.tensor_scalar(nmax[:, j % 8, :], top[:, j % 8, :, 0], -SCALE, None,
                                                ALU.mult).then_inc(nmax_done, 1)
                    if due(PROB, k, first, rest):
                        probabilities(T - 2 * PROB, (k - PROB) % PAIRS, first, k)
                    if first:
                        continue
                    if k - 1 in FFN_SLOTS:
                        n = (b - 1) * NF + FFN_SLOTS[k - 1] + 1
                        pool.wait_ge(hg_done, n)
                        pool.wait_ge(up_copied, n)
                        nc.gpsimd.tensor_tensor(hT[:, FFN_SLOTS[k - 1], :], hgs[:, :], ups[:, :],
                                                ALU.mult).then_inc(h_done, 1)
                    if k == OUT_PROJ + 2:
                        layer_norm(b, 0)
                    if k == DOWN + 4:
                        layer_norm(b, 1)

            nc.gpsimd.memset(minus_half[:, :], -0.5)
            nc.gpsimd.memset(half[:, :], 0.5).then_inc(half_set, 1)
            pool.wait_ge(half_set, 1)
            nc.gpsimd.memset(outs[:, :, :], 0.0).then_inc(stored, 16)
            pool.wait_ge(ffn_loaded, 16 * 5)
            for i, w in enumerate((wg, wu, wd)):
                nc.gpsimd.tensor_scalar(w[:, :, :].rearrange("p a n -> p (a n)"), wint[:, i, :], DEQ, None,
                                        ALU.mult).then_inc(deq_done, 1)
            slots(0, True, False)
            with pool.Fori(1, B) as b:
                slots(b, False, False)
            slots(B, False, True)


_INS = ["xT", "x", "wqT", "wkT", "wvT", "woT", "bq", "bk", "bv", "bo", "wgT", "wuT", "wdT", "ident", "ranks"]


def kernel(L0_attn_x, L0_attn_Wq, L0_attn_bq, L0_attn_Wk, L0_attn_bk, L0_attn_Wv, L0_attn_bv, L0_attn_Wo,
           L0_attn_bo, L0_ffn_w_gate, L0_ffn_w_up, L0_ffn_w_down):
    import concourse.bacc as _bacc
    from concourse.bass_utils import run_bass_kernel_spmd as _run

    laid_out = {
        "xT": L0_attn_x.transpose(0, 2, 1), "x": L0_attn_x,
        "wqT": L0_attn_Wq.T, "wkT": L0_attn_Wk.T, "wvT": L0_attn_Wv.T, "woT": L0_attn_Wo.T,
        "bq": L0_attn_bq.reshape(NG, HG, D).transpose(1, 2, 0), "bk": L0_attn_bk.reshape(NG, HG, D).transpose(1, 2, 0),
        "bv": L0_attn_bv.reshape(C, P).T, "bo": L0_attn_bo,
        "wgT": L0_ffn_w_gate.T, "wuT": L0_ffn_w_up.T, "wdT": L0_ffn_w_down.T,
        "ident": np.eye(P, dtype=np.float32),
        "ranks": np.tile(L - 2 * np.arange(TOP - 1, LEAST - 1, -1, dtype=np.float32), (P, 1)),
    }
    nc = _bacc.Bacc("TRN2", target_bir_lowering=False, num_devices=1)
    arrays, args = {}, []
    for name in _INS:
        a = np.ascontiguousarray(laid_out[name])
        arrays[f"in_{name}"] = a
        args.append(nc.dram_tensor(f"in_{name}", a.shape, mybir.dt.from_np(a.dtype), kind="ExternalInput").ap())
    out = nc.dram_tensor("out", (B, L, DM), F32, kind="ExternalOutput").ap()
    build(nc, *args, out)
    r = _run(nc, [arrays], core_ids=[0])
    return r.results[0]["out"]
```
